# Optimizing a Trainium2 kernel written in Bass

```python
import numpy as np
import jax
import jax.numpy as jnp

def _softmax(x, axis=-1):
    return jax.nn.softmax(x, axis=axis)
def _gelu(x):
    return jax.nn.gelu(x, approximate=True)
def _silu(x):
    return jax.nn.silu(x)
def _sigmoid(x):
    return jax.nn.sigmoid(x)
def _layernorm(x, axis=-1, eps=1e-5):
    m = jnp.mean(x, axis=axis, keepdims=True)
    v = jnp.var(x, axis=axis, keepdims=True)
    return (x - m) / jnp.sqrt(v + eps)
def _scatter_add(tgt, idx, src, axis=0):
    return tgt.at[idx].add(src)
def _segment_sum(src, seg, n):
    return jax.ops.segment_sum(src, seg, n)

kernel_name = 'mk_conv_seq_d1_conv_nhwc256_4235b1'

def setup_inputs(seed: int = 0):
    np.random.seed(seed)
    _w = jnp.asarray
    def _rec_inputs():
        import jax
        import jax.numpy as jnp
        _gk = jax.random.key(seed)
        x = -8.268e-05 + 0.9999 * jax.random.normal(jax.random.fold_in(_gk, 1), (64, 56, 56, 256), jnp.float32)
        return x
    x = _rec_inputs()
    def _L0_conv_setup():
        import jax, jax.numpy as jnp
        import numpy as np
        EPS = 1e-05
        M_PER_GROUP = 64
        ITER_NUM = 5

        def _iter_norm_whiten(x, gamma, beta):
            B, H, W, C = x.shape
            g = C // M_PER_GROUP
            m = M_PER_GROUP
            N = B * H * W
            xt = jnp.transpose(x, (3, 0, 1, 2)).reshape(C, N)
            mu = jnp.mean(xt, axis=1, keepdims=True)
            f = xt - mu
            fg = f.reshape(g, m, N)
            cov = jnp.einsum('gmn,gkn->gmk', fg, fg) / (jnp.float32(N) - 1.0)
            eye = jnp.eye(m, dtype=x.dtype)
            cov = (1.0 - EPS) * cov + EPS * eye
            trace = jnp.trace(cov, axis1=1, axis2=2)[:, None, None]
            sigma = cov / trace
            P = jnp.broadcast_to(eye, (g, m, m))
            for _ in range(ITER_NUM):
                P = (3.0 * P - P @ P @ P @ sigma) / 2.0
            wm = P / jnp.sqrt(trace)
            f_hat = jnp.einsum('gmk,gkn->gmn', wm, fg).reshape(C, B, H, W)
            out = jnp.transpose(f_hat, (1, 2, 3, 0))
            return gamma * out + beta
        key = jax.random.key(seed)
        k1, = jax.random.split(key, 1)
        x = jax.random.normal(k1, (64, 56, 56, 256), dtype=jnp.float32)
        gamma = jnp.ones((1, 1, 1, 256), dtype=jnp.float32)
        beta = jnp.zeros((1, 1, 1, 256), dtype=jnp.float32)
        return {'x': x, 'gamma': gamma, 'beta': beta}
    _L0_conv_all = _L0_conv_setup()
    _L0_conv_in = {k: v for k, v in _L0_conv_all.items() if k in ('gamma', 'beta', )}
    del _L0_conv_all

    return {
        "x": x,
        "L0_conv_gamma": _L0_conv_in["gamma"],
        "L0_conv_beta": _L0_conv_in["beta"],
    }

def reference(x, L0_conv_gamma, L0_conv_beta):
    import jax
    import jax.numpy as jnp
    def _L0_conv_ref(x, gamma, beta):
        import jax, jax.numpy as jnp
        import numpy as np
        EPS = 1e-05
        M_PER_GROUP = 64
        ITER_NUM = 5

        def _iter_norm_whiten(x, gamma, beta):
            B, H, W, C = x.shape
            g = C // M_PER_GROUP
            m = M_PER_GROUP
            N = B * H * W
            xt = jnp.transpose(x, (3, 0, 1, 2)).reshape(C, N)
            mu = jnp.mean(xt, axis=1, keepdims=True)
            f = xt - mu
            fg = f.reshape(g, m, N)
            cov = jnp.einsum('gmn,gkn->gmk', fg, fg) / (jnp.float32(N) - 1.0)
            eye = jnp.eye(m, dtype=x.dtype)
            cov = (1.0 - EPS) * cov + EPS * eye
            trace = jnp.trace(cov, axis1=1, axis2=2)[:, None, None]
            sigma = cov / trace
            P = jnp.broadcast_to(eye, (g, m, m))
            for _ in range(ITER_NUM):
                P = (3.0 * P - P @ P @ P @ sigma) / 2.0
            wm = P / jnp.sqrt(trace)
            f_hat = jnp.einsum('gmk,gkn->gmn', wm, fg).reshape(C, B, H, W)
            out = jnp.transpose(f_hat, (1, 2, 3, 0))
            return gamma * out + beta
        return _iter_norm_whiten(x, gamma, beta)

    def _gn(v, G=32, eps=1e-5):
        B_, H_, W_, C_ = v.shape
        g = v.reshape(B_, H_, W_, G, C_ // G)
        m = jnp.mean(g, axis=(1, 2, 4), keepdims=True)
        s = jnp.var(g, axis=(1, 2, 4), keepdims=True)
        return ((g - m) / jnp.sqrt(s + eps)).reshape(v.shape)

    def _ln_c(v, eps=1e-6):
        m = jnp.mean(v, axis=-1, keepdims=True)
        s = jnp.var(v, axis=-1, keepdims=True)
        return (v - m) / jnp.sqrt(s + eps)

    def _ln_t(v, eps=1e-5):
        m = jnp.mean(v, axis=-1, keepdims=True)
        s = jnp.var(v, axis=-1, keepdims=True)
        return (v - m) / jnp.sqrt(s + eps)

    def _to_tokens(v):
        B_, H_, W_, C_ = v.shape
        return v.reshape(B_, H_ * W_, C_)
    def _from_tokens(t, like):
        return t.reshape(like.shape)

    x = _L0_conv_ref(x, L0_conv_gamma, L0_conv_beta)
    return x


_drawn_inputs = setup_inputs


def setup_inputs(seed=0):
    import zlib

    import numpy as np

    out = dict(_drawn_inputs(seed))
    spreads = {'L0_conv_gamma': (1.0, 0.2), 'L0_conv_beta': (0.0, 0.1)}
    factors = {}
    for name, (base, spread) in spreads.items():
        noise = np.random.default_rng([zlib.crc32(name.encode()), seed]).standard_normal(out[name].shape)
        drawn = base * np.exp(spread * noise) if base else spread * noise
        out[name] = jnp.asarray(drawn.astype(out[name].dtype))
    for name, factor in factors.items():
        out[name] = (out[name] * factor).astype(out[name].dtype)
    return out
```

```python
import concourse.bass as bass
from concourse import mybir
from contextlib import ExitStack

FP32 = mybir.dt.float32
ALU = mybir.AluOpType
ACT = mybir.ActivationFunctionType
AX = mybir.AxisListType

P = 128
C = 256
M = 64
HALVES = C // P
PAIR = P // M
G = C // M
RP = 8
CHUNK = P * RP
RING = 4
KEPT = 12
DB = 2
YB = 4
RU = RP // 2
EPS = 1e-5
ITERATIONS = 5


def build(nc, x, gamma, beta, out):
    rows = x.shape[0] * x.shape[1] * x.shape[2]
    chunks = rows // CHUNK
    passed = chunks - KEPT
    streamed = passed - RING
    rounds = passed // RING
    laps = chunks // RING
    span = (chunks - RING) // KEPT
    assert chunks * CHUNK == rows and rounds * RING == passed and laps * RING == chunks
    assert span * KEPT == chunks - RING and span % RING == 0

    x_v = x.rearrange("b h w c -> (b h w) c").rearrange("(i p r) c -> i p (r c)", p=P, r=RP)
    out_v = out.rearrange("b h w c -> (b h w) c").rearrange("(i p r) c -> i p (r c)", p=P, r=RP)
    gamma_v = gamma.rearrange("a b c d -> (a b c) d")
    beta_v = beta.rearrange("a b c d -> (a b c) d")

    ctx = ExitStack()
    with ctx:
        def sb(name, shape):
            return ctx.enter_context(nc.sbuf_tensor(name, shape, FP32))

        def sem(name):
            return ctx.enter_context(nc.semaphore(name))

        ring = sb("ring", [P, RING, RP * C])
        kept = sb("kept", [P, KEPT, RP * C])
        work = sb("work", [P, YB * RP * C])
        shifted = work[:, 0:DB * RP * HALVES * (P + 1)].rearrange("p (j r b n) -> p j r b n", j=DB, r=RP, b=HALVES)
        y = work[:, :].rearrange("p (s n) -> p s n", s=YB)
        zT = sb("zT", [P, 2, HALVES, RU * P])
        ident = sb("ident", [P, P])
        identc = sb("identc", [P, HALVES, M])
        eps_ident = sb("eps_ident", [P, HALVES, M])
        ident15 = sb("ident15", [P, HALVES, P])
        same_group = sb("same_group", [P, P])
        averager = sb("averager", [P, P])
        gamma_all = sb("gamma_all", [P, C])
        beta_all = sb("beta_all", [P, RU, C])
        shift = sb("shift", [P, C])
        shift_diag = sb("shift_diag", [P, HALVES, P])
        shift_col = sb("shift_col", [P, HALVES])
        moments = sb("moments", [P, HALVES, M + 1])
        sum_diag = sb("sum_diag", [P, HALVES, M])
        mean_col = sb("mean_col", [P, HALVES])
        neg_mean = sb("neg_mean", [P, HALVES])
        cov = sb("cov", [P, HALVES, M])
        cov_diag = sb("cov_diag", [P, HALVES, M])
        trace_part = sb("trace_part", [P, HALVES])
        trace = sb("trace", [P, HALVES])
        inv_trace = sb("inv_trace", [P, HALVES])
        root = sb("root", [P, HALVES])
        newton = sb("newton", [P, 3, HALVES])
        inv_root = sb("inv_root", [P, HALVES])
        sigma = sb("sigma", [P, HALVES, P])
        white = sb("white", [P, HALVES, P])
        white15 = sb("white15", [P, HALVES, P])
        products = sb("products", [P, 2, HALVES, P])
        weights = sb("weights", [P, HALVES, P])

        banks = ctx.enter_context(nc.psum_tensor("banks", [P, 8, 512], FP32))
        xT_ps = banks[:, 0:4, :].rearrange("p (u b) n -> p u b n", u=2)
        y_ps = banks[:, 4:8, :].rearrange("p (u v) n -> p u (v n)", u=2)
        moments_ps = banks[:, 4:6, 0:P + 1]
        shift_ps = banks[:, 6, 0:C]
        sums_ps = banks[:, 6, 0:P].rearrange("p (b m) -> p b m", b=HALVES)
        trace_ps = banks[:, 7, 0:HALVES]
        products_ps = banks[:, 6, :].rearrange("p (k b n) -> p k b n", k=2, b=HALVES)
        cubic_ps = banks[:, 7, 0:HALVES * P].rearrange("p (b n) -> p b n", b=HALVES)

        ring_loaded = [sem(f"ring_loaded{s}") for s in range(RING)]
        kept_loaded = [sem(f"kept_loaded{k}") for k in range(KEPT)]
        params_loaded = sem("params_loaded")
        consts_ready = sem("consts_ready")
        shift_summed = sem("shift_summed")
        rows_shifted = sem("rows_shifted")
        rows_used = sem("rows_used")
        sum_diag_ready = sem("sum_diag_ready")
        sums_spread = sem("sums_spread")
        trace_part_ready = sem("trace_part_ready")
        trace_summed = sem("trace_summed")
        trace_ready = sem("trace_ready")
        root_ready = sem("root_ready")
        mean_ready = sem("mean_ready")
        white_ready = sem("white_ready")
        products_done = sem("products_done")
        products_copied = sem("products_copied")
        cubic_done = sem("cubic_done")
        weights_ready = sem("weights_ready")
        chain = sem("chain")
        xT_done = sem("xT_done")
        zT_ready = sem("zT_ready")
        y_summed = sem("y_summed")
        y_ready = sem("y_ready")
        y_stored = [sem(f"y_stored{s}") for s in range(YB)]

        block = ctx.enter_context(nc.Block())

        @block.sync
        def _(sp):
            for s in range(RING):
                sp.dma_start(ring[:, s, :], x_v[s]).then_inc(ring_loaded[s], 16)
            sp.dma_start(gamma_all[:, :], gamma_v.partition_broadcast(P)).then_inc(params_loaded, 16)
            for r in range(RU):
                sp.dma_start(beta_all[:, r, :], beta_v.partition_broadcast(P)).then_inc(params_loaded, 16)
            with sp.Fori(1, rounds) as k:
                for s in range(RING):
                    sp.wait_ge(rows_shifted, k * RING + (s - RING + 1))
                    sp.dma_start(ring[:, s, :], x_v[k * RING + s]).then_inc(ring_loaded[s], 16)
            for c in range(KEPT):
                sp.dma_start(kept[:, c, :], x_v[passed + c]).then_inc(kept_loaded[c], 16)

            def store(position, s, chunk):
                sp.wait_ge(y_ready, 2 * position + 2)
                sp.dma_start(out_v[chunk], y[:, s % YB, :]).then_inc(y_stored[s % YB], 16)

            def load(position, s, chunk):
                sp.wait_ge(xT_done, 2 * (position - RING + 1))
                sp.dma_start(ring[:, s, :], x_v[chunk]).then_inc(ring_loaded[s], 16)

            for s in range(RING):
                load(RING + s, s, s)
                store(s, s, streamed + s)
            with sp.Fori(0, KEPT - 1) as run:
                for j in range(span):
                    ahead = j + RING
                    if ahead < span - 1:
                        load(run * span + (RING + ahead), ahead % RING, run * (span - 1) + ahead)
                    elif ahead >= span:
                        load(run * span + (RING + ahead), ahead % RING,
                             run * (span - 1) + (span - 1 + ahead - span))
                    store(run * span + (RING + j), j % RING,
                          run * (span - 1) + j if j < span - 1 else run + (passed))
            last = KEPT - 1
            for j in range(span):
                ahead = j + RING
                if ahead < span - 1:
                    load(last * span + RING + ahead, ahead % RING, last * (span - 1) + ahead)
                store(last * span + RING + j, j % RING,
                      last * (span - 1) + j if j < span - 1 else last + passed)
            for s in range(YB):
                sp.wait_ge(y_stored[s], 16 * (chunks // YB))

        consts = 1 + DB + 4 + PAIR + HALVES * (1 + 2 * PAIR)

        @block.gpsimd
        def _(pool):
            made = [0]

            def make(ins):
                made[0] += 1
                ins.then_inc(consts_ready, 1)
                pool.wait_ge(consts_ready, made[0])

            make(pool.memset(averager[:, :], 1.0 / CHUNK))
            for j in range(DB):
                make(pool.memset(shifted[:, j, :, :, P:P + 1], 1.0))
            make(pool.memset(ident[:, :], 0.0))
            make(pool.affine_select(out=ident[:, :], in_=ident[:, :], compare_op=ALU.not_equal, fill=1.0,
                                    base=0, pattern=[[-1, P]], channel_multiplier=1))
            make(pool.memset(sigma[:, :, :], 0.0))
            make(pool.memset(same_group[:, :], 0.0))
            for h in range(PAIR):
                block_h = slice(h * M, (h + 1) * M)
                make(pool.memset(same_group[block_h, block_h], 1.0))
            for b in range(HALVES):
                make(pool.tensor_scalar(ident15[:, b, :], ident[:, :], 1.5, None, ALU.mult))
            for h in range(PAIR):
                block_h = slice(h * M, (h + 1) * M)
                for b in range(HALVES):
                    make(pool.tensor_scalar(identc[block_h, b, :], ident[block_h, block_h], 1.0, None, ALU.mult))
                    make(pool.tensor_scalar(eps_ident[block_h, b, :], ident[block_h, block_h], EPS, None,
                                            ALU.mult))
            assert made[0] == consts
            for c in range(KEPT):
                position = RING + (c + 1) * span - 1
                s = position % RING
                pool.wait_ge(kept_loaded[c], 16)
                pool.wait_ge(xT_done, 2 * (position - RING + 1))
                pool.tensor_copy(ring[:, s, :], kept[:, c, :]).then_inc(ring_loaded[s], 16)

        @block.scalar
        def _(act):
            act.wait_ge(trace_ready, 1)
            nc.scalar.activation(root[:, :], trace[:, :], ACT.Sqrt).then_inc(root_ready, 1)
            act.wait_ge(mean_ready, 1)

            def center(unit, u, first):
                act.wait_ge(xT_done, unit + 1)
                if not first:
                    act.wait_ge(y_summed, unit - 1)
                for b in range(HALVES):
                    last = nc.scalar.activation(zT[:, u, b, :], xT_ps[:, u, b, :], ACT.Identity,
                                                bias=neg_mean[:, b:b + 1])
                last.then_inc(zT_ready, 1)

            for unit in range(2 * RING):
                center(unit, unit % 2, unit < 2)
            with act.Fori(1, laps) as k:
                for j in range(2 * RING):
                    center(k * (2 * RING) + j, j % 2, False)

        @block.vector
        def _(dve):
            links = [0]

            def link(ins):
                links[0] += 1
                ins.then_inc(chain, 1)
                dve.wait_ge(chain, links[0])

            dve.wait_ge(shift_summed, 1)
            link(nc.vector.tensor_copy(shift[:, :], shift_ps))
            dve.wait_ge(consts_ready, consts)
            shift_r = shift[:, :].rearrange("p (b n) -> p b n", b=HALVES).unsqueeze(1).to_broadcast([P, RP, HALVES, P])

            def shift_rows(source, j):
                nc.vector.tensor_tensor(shifted[:, j, :, :, 0:P],
                                        source.rearrange("p (r b n) -> p r b n", r=RP, b=HALVES),
                                        shift_r, ALU.subtract).then_inc(rows_shifted, 1)

            for s in range(RING):
                dve.wait_ge(ring_loaded[s], 16)
                if s >= DB:
                    dve.wait_ge(rows_used, s - DB + 1)
                shift_rows(ring[:, s, :], s % DB)
            link(nc.vector.tensor_tensor(shift_diag[:, :, :], shift[:, :].rearrange("p (b n) -> p b n", b=HALVES),
                                         ident[:, :].unsqueeze(1).to_broadcast([P, HALVES, P]), ALU.mult))
            link(nc.vector.tensor_reduce(shift_col[:, :], shift_diag[:, :, :], AX.X, ALU.add))
            with dve.Fori(1, rounds) as k:
                for s in range(RING):
                    dve.wait_ge(ring_loaded[s], k * 16 + 16)
                    dve.wait_ge(rows_used, k * RING + (s - DB + 1))
                    shift_rows(ring[:, s, :], s % DB)
            for c in range(KEPT):
                dve.wait_ge(kept_loaded[c], 16)
                dve.wait_ge(rows_used, passed + c - DB + 1)
                shift_rows(kept[:, c, :], c % DB)

            dve.wait_ge(rows_used, chunks)
            for h in range(PAIR):
                block_h = slice(h * M, (h + 1) * M)
                nc.vector.tensor_copy(moments[block_h, :, 0:M], moments_ps[block_h, :, block_h])
            link(nc.vector.tensor_copy(moments[:, :, M], moments_ps[:, :, P]))
            nc.vector.tensor_tensor(sum_diag[:, :, :], identc[:, :, :],
                                    moments[:, :, M:M + 1].to_broadcast([P, HALVES, M]),
                                    ALU.mult).then_inc(sum_diag_ready, 1)
            nc.vector.scalar_tensor_tensor(out=neg_mean[:, :], in0=moments[:, :, M], scalar=-1.0 / rows,
                                           in1=shift_col[:, :], op0=ALU.mult,
                                           op1=ALU.subtract).then_inc(mean_ready, 1)
            link(nc.vector.tensor_scalar(mean_col[:, :], moments[:, :, M], 1.0 / rows, None, ALU.mult))
            dve.wait_ge(sums_spread, 1)
            for b in range(HALVES):
                last = nc.vector.scalar_tensor_tensor(out=cov[:, b, :], in0=sums_ps[:, b, :],
                                                      scalar=mean_col[:, b:b + 1], in1=moments[:, b, 0:M],
                                                      op0=ALU.mult, op1=ALU.subtract)
            link(last)
            link(nc.vector.scalar_tensor_tensor(out=cov[:, :, :], in0=cov[:, :, :],
                                                scalar=-(1.0 - EPS) / (rows - 1.0), in1=eps_ident[:, :, :],
                                                op0=ALU.mult, op1=ALU.add))
            link(nc.vector.tensor_tensor(cov_diag[:, :, :], cov[:, :, :], identc[:, :, :], ALU.mult))
            nc.vector.tensor_reduce(trace_part[:, :], cov_diag[:, :, :], AX.X,
                                    ALU.add).then_inc(trace_part_ready, 1)
            dve.wait_ge(trace_summed, 1)
            nc.vector.tensor_copy(trace[:, :], trace_ps).then_inc(trace_ready, 1)
            dve.wait_ge(trace_ready, 1)
            link(nc.vector.reciprocal(inv_trace[:, :], trace[:, :]))
            for h in range(PAIR):
                block_h = slice(h * M, (h + 1) * M)
                last = nc.vector.tensor_tensor(sigma[block_h, :, block_h], cov[block_h, :, :],
                                               inv_trace[block_h, :].unsqueeze(2).to_broadcast([M, HALVES, M]),
                                               ALU.mult)
            link(last)

            nc.vector.scalar_tensor_tensor(out=white[:, :, :], in0=sigma[:, :, :], scalar=-0.5,
                                           in1=ident15[:, :, :], op0=ALU.mult,
                                           op1=ALU.add).then_inc(white_ready, 1)
            for t in range(1, ITERATIONS):
                dve.wait_ge(white_ready, t)
                link(nc.vector.tensor_scalar(white15[:, :, :], white[:, :, :], 1.5, None, ALU.mult))
                if t == 1:
                    dve.wait_ge(root_ready, 1)
                    link(nc.vector.reciprocal(newton[:, 0, :], root[:, :]))
                    link(nc.vector.tensor_tensor(newton[:, 1, :], newton[:, 0, :], trace[:, :], ALU.mult))
                    link(nc.vector.tensor_tensor(newton[:, 2, :], newton[:, 1, :], root[:, :], ALU.add))
                    link(nc.vector.tensor_scalar(newton[:, 2, :], newton[:, 2, :], 0.5, None, ALU.mult))
                    link(nc.vector.reciprocal(inv_root[:, :], newton[:, 2, :]))
                dve.wait_ge(products_done, t)
                nc.vector.tensor_copy(products[:, :, :, :], products_ps).then_inc(products_copied, 1)
                dve.wait_ge(cubic_done, t)
                nc.vector.scalar_tensor_tensor(out=white[:, :, :], in0=cubic_ps, scalar=-0.5,
                                               in1=white15[:, :, :], op0=ALU.mult,
                                               op1=ALU.add).then_inc(white_ready, 1)
            dve.wait_ge(white_ready, ITERATIONS)
            dve.wait_ge(params_loaded, 16 * (1 + RU))
            for b in range(HALVES):
                last = nc.vector.scalar_tensor_tensor(out=weights[:, b, :], in0=white[:, b, :],
                                                      scalar=inv_root[:, b:b + 1],
                                                      in1=gamma_all[:, b * P:(b + 1) * P],
                                                      op0=ALU.mult, op1=ALU.mult)
            last.then_inc(weights_ready, 1)

            def finish(unit, u, s, part, stores):
                dve.wait_ge(y_summed, unit + 1)
                if part == 0 and stores is not None:
                    dve.wait_ge(y_stored[s], stores)
                nc.vector.tensor_tensor(y[:, s, part * RU * C:(part + 1) * RU * C], y_ps[:, u, :],
                                        beta_all[:, :, :].rearrange("p r c -> p (r c)"),
                                        ALU.add).then_inc(y_ready, 1)

            for unit in range(2 * RING):
                finish(unit, unit % 2, unit // 2, unit % 2, None)
            with dve.Fori(1, laps) as k:
                for j in range(2 * RING):
                    finish(k * (2 * RING) + j, j % 2, j // 2, j % 2, k * 16)

        @block.tensor
        def _(pe):
            pe.wait_ge(consts_ready, 1)
            pe.wait_ge(ring_loaded[0], 16)
            for r in range(RP):
                last = nc.tensor.matmul(shift_ps, averager[:, :], ring[:, 0, r * C:(r + 1) * C],
                                        start=(r == 0), stop=(r == RP - 1))
            last.then_inc(shift_summed, 1)

            def accumulate(j, first, final):
                for r in range(RP):
                    for b in range(HALVES):
                        last = nc.tensor.matmul(moments_ps[:, b, :], shifted[:, j, r, b, 0:P],
                                                shifted[:, j, r, b, :], start=(first and r == 0),
                                                stop=(final and r == RP - 1))
                last.then_inc(rows_used, 1)

            for j in range(RING):
                pe.wait_ge(rows_shifted, j + 1)
                accumulate(j % DB, j == 0, False)
            with pe.Fori(1, chunks // RING - 1) as k:
                for j in range(RING):
                    pe.wait_ge(rows_shifted, k * RING + (j + 1))
                    accumulate(j % DB, False, False)
            for j in range(RING):
                pe.wait_ge(rows_shifted, chunks - RING + j + 1)
                accumulate(j % DB, False, j == RING - 1)

            def transpose_unit(unit, u, s, part, loads, first):
                if part == 0:
                    pe.wait_ge(ring_loaded[s], loads)
                if not first:
                    pe.wait_ge(zT_ready, unit - 1)
                for r in range(RU):
                    for b in range(HALVES):
                        col = (part * RU + r) * C + b * P
                        last = nc.tensor.transpose(xT_ps[:, u, b, r * P:(r + 1) * P],
                                                   ring[:, s, col:col + P], ident[:, :])
                last.then_inc(xT_done, 1)

            def multiply_unit(unit, u, first):
                pe.wait_ge(zT_ready, unit + 1)
                if not first:
                    pe.wait_ge(y_ready, unit - 1)
                for r in range(RU):
                    for b in range(HALVES):
                        col = r * C + b * P
                        last = nc.tensor.matmul(y_ps[:, u, col:col + P], zT[:, u, b, r * P:(r + 1) * P],
                                                weights[:, b, :], start=True, stop=True)
                last.then_inc(y_summed, 1)

            pe.wait_ge(consts_ready, consts)
            transpose_unit(0, 0, 0, 0, 16 * rounds, True)

            pe.wait_ge(sum_diag_ready, 1)
            nc.tensor.matmul(sums_ps.rearrange("p b m -> p (b m)"), same_group[:, :],
                             sum_diag[:, :, :].rearrange("p b m -> p (b m)"),
                             start=True, stop=True).then_inc(sums_spread, 1)
            pe.wait_ge(trace_part_ready, 1)
            nc.tensor.matmul(trace_ps, same_group[:, :], trace_part[:, :],
                             start=True, stop=True).then_inc(trace_summed, 1)
            for t in range(1, ITERATIONS):
                pe.wait_ge(white_ready, t)
                for b in range(HALVES):
                    nc.tensor.matmul(products_ps[:, 0, b, :], white[:, b, :], white[:, b, :],
                                     start=True, stop=True)
                    last = nc.tensor.matmul(products_ps[:, 1, b, :], white[:, b, :], sigma[:, b, :],
                                            start=True, stop=True)
                last.then_inc(products_done, 1)
                pe.wait_ge(products_copied, t)
                for b in range(HALVES):
                    last = nc.tensor.matmul(cubic_ps[:, b, :], products[:, 0, b, :], products[:, 1, b, :],
                                            start=True, stop=True)
                last.then_inc(cubic_done, 1)
            pe.wait_ge(weights_ready, 1)

            def lap(k, first, final):
                for j in range(2 * RING):
                    n = j + 1
                    ahead = k * (2 * RING) + n
                    s, part = (n // 2) % RING, n % 2
                    if not (final and n == 2 * RING):
                        transpose_unit(ahead, n % 2, s, part,
                                       k * 16 + 16 * (rounds + n // (2 * RING)), first and n < 2)
                    multiply_unit(k * (2 * RING) + j, j % 2, first and j < 2)

            lap(0, True, False)
            with pe.Fori(1, laps - 1) as k:
                lap(k, False, False)
            lap(laps - 1, False, True)


def kernel(x, L0_conv_gamma, L0_conv_beta):
    import numpy as _np
    import concourse.bacc as _bacc
    from concourse import mybir as _mybir
    from concourse.bass_utils import run_bass_kernel_spmd as _run

    nc = _bacc.Bacc("TRN2", target_bir_lowering=False, num_devices=1)
    arrays, args = {}, []
    for name, value in (("x", x), ("gamma", L0_conv_gamma), ("beta", L0_conv_beta)):
        a = _np.ascontiguousarray(value)
        arrays[name] = a
        args.append(nc.dram_tensor(name, a.shape, _mybir.dt.from_np(a.dtype), kind="ExternalInput").ap())
    args.append(nc.dram_tensor("out", arrays["x"].shape, _mybir.dt.float32, kind="ExternalOutput").ap())
    build(nc, *args)
    r = _run(nc, [arrays], core_ids=[0])
    return r.results[0]["out"]
```

```python
import concourse.bass as bass
from concourse import mybir
from contextlib import ExitStack

FP32 = mybir.dt.float32
FP32R = mybir.dt.float32r
BF16 = mybir.dt.bfloat16
INT32 = mybir.dt.int32
ALU = mybir.AluOpType
ACT = mybir.ActivationFunctionType
AX = mybir.AxisListType

P = 128
C = 256
M = 64
HALVES = C // P
PAIR = P // M
G = C // M
RP = 8
CHUNK = P * RP
RING = 4
KEPT = 12
UB = 3
UNITS = 2
YB = 4
RU = RP // UNITS
SAMPLE = 2
OFFSET = 16.0
EPS = 1e-5
ITERATIONS = 5


def build(nc, x, gamma, beta, out):
    rows = x.shape[0] * x.shape[1] * x.shape[2]
    chunks = rows // CHUNK
    passed = chunks - KEPT
    streamed = passed - RING
    rounds = passed // RING
    units = UNITS * chunks
    lap_units = UNITS * RING
    head_units = UNITS * KEPT + lap_units
    laps = chunks // RING
    span = (chunks - RING) // KEPT
    assert (rounds - 1) % UB == 0 and head_units % UB == 2 and (units - 2) % UB == 0
    assert chunks * CHUNK == rows and rounds * RING == passed and laps * RING == chunks
    assert span * KEPT == chunks - RING and span % RING == 0

    x_v = x.rearrange("b h w c -> (b h w) c").rearrange("(i p r) c -> i p (r c)", p=P, r=RP)
    out_v = out.rearrange("b h w c -> (b h w) c").rearrange("(i p r) c -> i p (r c)", p=P, r=RP)
    gamma_v = gamma.rearrange("a b c d -> (a b c) d")
    beta_v = beta.rearrange("a b c d -> (a b c) d")

    ctx = ExitStack()
    with ctx:
        def sb(name, shape, dtype=FP32):
            return ctx.enter_context(nc.sbuf_tensor(name, shape, dtype))

        def sem(name):
            return ctx.enter_context(nc.semaphore(name))

        ring = sb("ring", [P, RING, RP * C])
        kept = sb("kept", [P, KEPT, RP * C])
        work = sb("work", [P, YB * RP * C])
        shifted_size = UB * RU * HALVES * (P + 1)
        shifted = work[:, 0:shifted_size].rearrange("p (u r b n) -> p u r b n", u=UB, r=RU, b=HALVES)
        squares = work[:, shifted_size:shifted_size + SAMPLE * C]
        y = work[:, :].rearrange("p (s n) -> p s n", s=YB)
        carved = [shifted_size + SAMPLE * C]

        def scratch(shape):
            first, size = carved[0], shape[1] * shape[2]
            carved[0] += size
            assert carved[0] <= YB * RP * C
            return work[:, first:first + size].rearrange("p (a b) -> p a b", b=shape[2])

        parts = sb("parts", [P, UB, RU, HALVES, 2 * P + 2], FP32R)
        low_bf16 = parts[:, :, :, :, :].bitcast(BF16).rearrange("p u r b (n t) -> p u r b n t", t=2)[:, :, :, :, P:, 1]
        zT = sb("zT", [P, 2, HALVES, RU * P])
        ident = sb("ident", [P, P])
        identc = sb("identc", [P, HALVES, M])
        eps_ident = sb("eps_ident", [P, HALVES, M])
        ident15 = sb("ident15", [P, HALVES, P])
        same_group = sb("same_group", [P, P])
        averager = sb("averager", [P, P])
        gamma_all = sb("gamma_all", [P, C])
        beta_all = sb("beta_all", [P, C])
        sampled = sb("sampled", [P, 2, C])
        shift = sampled[:, 0, :]
        mean_sq = sb("mean_sq", [P, C])
        margin = sb("margin", [P, C])
        least_margin = sb("least_margin", [P, 1])
        near_zero = sb("near_zero", [P, 1], INT32)
        cross_half = scratch([P, HALVES, P])
        cross = scratch([P, HALVES, P])
        high_sum = sb("high_sum", [P, HALVES])
        shift_diag = scratch([P, HALVES, P])
        shift_col = sb("shift_col", [P, HALVES])
        moments = sb("moments", [P, HALVES, M + 1])
        sum_diag = scratch([P, HALVES, M])
        mean_col = sb("mean_col", [P, HALVES])
        neg_mean = sb("neg_mean", [P, HALVES])
        cov = scratch([P, HALVES, M])
        cov_diag = scratch([P, HALVES, M])
        trace_part = sb("trace_part", [P, HALVES])
        trace = sb("trace", [P, HALVES])
        inv_trace = sb("inv_trace", [P, HALVES])
        root = sb("root", [P, HALVES])
        newton = sb("newton", [P, 3, HALVES])
        inv_root = sb("inv_root", [P, HALVES])
        sigma = scratch([P, HALVES, P])
        white = scratch([P, HALVES, P])
        white15 = scratch([P, HALVES, P])
        products = scratch([P, 2 * HALVES, P]).rearrange("p (k b) n -> p k b n", k=2)
        weights = sb("weights", [P, HALVES, P])

        banks = ctx.enter_context(nc.psum_tensor("banks", [P, 8, 512], FP32))
        xT_ps = banks[:, 0:4, :].rearrange("p (u b) n -> p u b n", u=2)
        y_ps = banks[:, 4:8, :].rearrange("p (u v) n -> p u (v n)", u=2)
        moments_ps = banks[:, 4:6, 0:P + 1]
        cross_ps = banks[:, 6:8, 0:2 * P + 2]
        sampled_ps = banks[:, 2:4, 0:C]
        sums_ps = banks[:, 6, 0:P].rearrange("p (b m) -> p b m", b=HALVES)
        trace_ps = banks[:, 7, 0:HALVES]
        products_ps = banks[:, 6, :].rearrange("p (k b n) -> p k b n", k=2, b=HALVES)
        cubic_ps = banks[:, 7, 0:HALVES * P].rearrange("p (b n) -> p b n", b=HALVES)

        ring_loaded = [sem(f"ring_loaded{s}") for s in range(RING)]
        kept_loaded = [sem(f"kept_loaded{k}") for k in range(KEPT)]
        params_loaded = sem("params_loaded")
        consts_ready = sem("consts_ready")
        squared = sem("squared")
        sample_summed = sem("sample_summed")
        way_chosen = sem("way_chosen")
        high_ready = sem("high_ready")
        rows_ready = sem("rows_ready")
        rows_used = sem("rows_used")
        shift_diag_ready = sem("shift_diag_ready")
        half_ready = sem("half_ready")
        cross_ready = sem("cross_ready")
        cross_added = sem("cross_added")
        offsets_ready = sem("offsets_ready")
        sum_diag_ready = sem("sum_diag_ready")
        sums_spread = sem("sums_spread")
        trace_part_ready = sem("trace_part_ready")
        trace_summed = sem("trace_summed")
        trace_ready = sem("trace_ready")
        root_ready = sem("root_ready")
        mean_ready = sem("mean_ready")
        white_ready = sem("white_ready")
        products_done = sem("products_done")
        products_copied = sem("products_copied")
        cubic_done = sem("cubic_done")
        weights_ready = sem("weights_ready")
        chain = sem("chain")
        xT_done = sem("xT_done")
        zT_ready = sem("zT_ready")
        y_summed = sem("y_summed")
        y_ready = sem("y_ready")
        y_stored = [sem(f"y_stored{s}") for s in range(YB)]

        block = ctx.enter_context(nc.Block())

        @block.sync
        def _(sp):
            for c in range(KEPT):
                sp.dma_start(kept[:, c, :], x_v[c]).then_inc(kept_loaded[c], 16)
            for s in range(RING):
                sp.dma_start(ring[:, s, :], x_v[KEPT + s]).then_inc(ring_loaded[s], 16)
            sp.dma_start(gamma_all[:, :], gamma_v.partition_broadcast(P)).then_inc(params_loaded, 16)
            sp.dma_start(beta_all[:, :], beta_v.partition_broadcast(P)).then_inc(params_loaded, 16)
            with sp.Fori(1, rounds) as k:
                for s in range(RING):
                    sp.wait_ge(rows_ready, k * lap_units + UNITS * (KEPT - RING + s + 1))
                    sp.dma_start(ring[:, s, :], x_v[k * RING + (KEPT + s)]).then_inc(ring_loaded[s], 16)

            def store(position, s, chunk):
                sp.wait_ge(y_ready, 2 * position + 2)
                sp.dma_start(out_v[chunk], y[:, s % YB, :]).then_inc(y_stored[s % YB], 16)

            def load(position, s, chunk):
                sp.wait_ge(xT_done, 2 * (position - RING + 1))
                sp.dma_start(ring[:, s, :], x_v[chunk]).then_inc(ring_loaded[s], 16)

            for s in range(RING):
                load(RING + s, s, KEPT + s)
                store(s, s, chunks - RING + s)
            with sp.Fori(0, KEPT - 1) as run:
                for j in range(span):
                    ahead = j + RING
                    if ahead < span - 1:
                        load(run * span + (RING + ahead), ahead % RING,
                             run * (span - 1) + (KEPT + ahead))
                    elif ahead >= span:
                        load(run * span + (RING + ahead), ahead % RING,
                             run * (span - 1) + (KEPT + span - 1 + ahead - span))
                    store(run * span + (RING + j), j % RING,
                          run * (span - 1) + (KEPT + j) if j < span - 1 else run)
            last = KEPT - 1
            for j in range(span):
                ahead = j + RING
                if ahead < span - 1:
                    load(last * span + RING + ahead, ahead % RING,
                         KEPT + last * (span - 1) + ahead)
                store(last * span + RING + j, j % RING,
                      KEPT + last * (span - 1) + j if j < span - 1 else last)
            for s in range(YB):
                sp.wait_ge(y_stored[s], 16 * (chunks // YB))

        consts = 1 + 2 * UB + 4 + PAIR + HALVES * (1 + 2 * PAIR)

        @block.gpsimd
        def _(pool):
            made = [0]

            def make(ins):
                made[0] += 1
                ins.then_inc(consts_ready, 1)
                pool.wait_ge(consts_ready, made[0])

            make(pool.memset(averager[:, :], 1.0 / (P * SAMPLE)))
            for u in range(UB):
                make(pool.memset(parts[:, u, :, :, 2 * P:].bitcast(FP32), 1.0))
                make(pool.memset(shifted[:, u, :, :, P:], 1.0))
            make(pool.memset(ident[:, :], 0.0))
            make(pool.affine_select(out=ident[:, :], in_=ident[:, :], compare_op=ALU.not_equal, fill=1.0,
                                    base=0, pattern=[[-1, P]], channel_multiplier=1))
            make(pool.memset(sigma[:, :, :], 0.0))
            make(pool.memset(same_group[:, :], 0.0))
            for h in range(PAIR):
                block_h = slice(h * M, (h + 1) * M)
                make(pool.memset(same_group[block_h, block_h], 1.0))
            for b in range(HALVES):
                make(pool.tensor_scalar(ident15[:, b, :], ident[:, :], 1.5, None, ALU.mult))
            for h in range(PAIR):
                block_h = slice(h * M, (h + 1) * M)
                for b in range(HALVES):
                    make(pool.tensor_scalar(identc[block_h, b, :], ident[block_h, block_h], 1.0, None, ALU.mult))
                    make(pool.tensor_scalar(eps_ident[block_h, b, :], ident[block_h, block_h], EPS, None,
                                            ALU.mult))
            assert made[0] == consts
            for c in range(KEPT):
                position = RING + (c + 1) * span - 1
                s = position % RING
                pool.wait_ge(kept_loaded[c], 16)
                pool.wait_ge(xT_done, 2 * (position - RING + 1))
                pool.tensor_copy(ring[:, s, :], kept[:, c, :]).then_inc(ring_loaded[s], 16)

        @block.scalar
        def _(act):
            act.wait_ge(kept_loaded[0], 16)
            nc.scalar.activation(squares, kept[:, 0, 0:SAMPLE * C], ACT.Square).then_inc(squared, 1)

            def split_high(unit, u, source, first):
                if not first:
                    act.wait_ge(rows_used, unit - (UB - 1))
                nc.scalar.activation(parts[:, u, :, :, 0:P],
                                     source.rearrange("p (r b n) -> p r b n", r=RU, b=HALVES),
                                     ACT.Copy).then_inc(high_ready, 1)

            act.wait_ge(way_chosen, 1)
            with act.If(act.value_load(near_zero[0:1, 0:1], min_val=0, max_val=1) == 1):
                for unit in range(UNITS * KEPT):
                    c, part = unit // UNITS, unit % UNITS
                    act.wait_ge(kept_loaded[c], 16)
                    split_high(unit, unit % UB, kept[:, c, part * RU * C:(part + 1) * RU * C], unit < UB)
                for j in range(lap_units):
                    s, part = j // UNITS, j % UNITS
                    act.wait_ge(ring_loaded[s], 16)
                    split_high(UNITS * KEPT + j, (UNITS * KEPT + j) % UB,
                               ring[:, s, part * RU * C:(part + 1) * RU * C], False)
                with act.Fori(0, (rounds - 1) // UB) as k:
                    for j in range(UB * lap_units):
                        s, part, lap = j // UNITS % RING, j % UNITS, j // lap_units
                        act.wait_ge(ring_loaded[s], k * (16 * UB) + 16 * (lap + 2))
                        split_high(k * (UB * lap_units) + (head_units + j), (head_units + j) % UB,
                                   ring[:, s, part * RU * C:(part + 1) * RU * C], False)

            act.wait_ge(trace_ready, 1)
            nc.scalar.activation(root[:, :], trace[:, :], ACT.Sqrt).then_inc(root_ready, 1)
            act.wait_ge(mean_ready, 1)

            def center(unit, u, first):
                act.wait_ge(xT_done, unit + 1)
                if not first:
                    act.wait_ge(y_summed, unit - 1)
                for b in range(HALVES):
                    last = nc.scalar.activation(zT[:, u, b, :], xT_ps[:, u, b, :], ACT.Identity,
                                                bias=neg_mean[:, b:b + 1])
                last.then_inc(zT_ready, 1)

            for unit in range(2 * RING):
                center(unit, unit % 2, unit < 2)
            with act.Fori(1, laps) as k:
                for j in range(2 * RING):
                    center(k * (2 * RING) + j, j % 2, False)

        @block.vector
        def _(dve):
            links = [0]

            def link(ins):
                links[0] += 1
                ins.then_inc(chain, 1)
                dve.wait_ge(chain, links[0])

            dve.wait_ge(sample_summed, 1)
            link(nc.vector.tensor_copy(sampled[:, :, :], sampled_ps))
            link(nc.vector.tensor_tensor(mean_sq[:, :], shift, shift, ALU.mult))
            link(nc.vector.tensor_scalar(mean_sq[:, :], mean_sq[:, :], 1.0 + OFFSET, None, ALU.mult))
            link(nc.vector.scalar_tensor_tensor(out=margin[:, :], in0=sampled[:, 1, :], scalar=OFFSET,
                                                in1=mean_sq[:, :], op0=ALU.mult, op1=ALU.subtract))
            link(nc.vector.tensor_reduce(least_margin[:, :], margin[:, :], AX.X, ALU.min))
            nc.vector.tensor_scalar(near_zero[:, :], least_margin[:, :], 0.0, None, ALU.is_ge)\
                .then_inc(way_chosen, 1)

            def split_low(unit, u, source):
                dve.wait_ge(high_ready, unit + 1)
                nc.vector.tensor_tensor(parts[:, u, :, :, P:2 * P],
                                        source.rearrange("p (r b n) -> p r b n", r=RU, b=HALVES),
                                        parts[:, u, :, :, 0:P], ALU.subtract).then_inc(rows_ready, 1)

            shift_r = shift.rearrange("p (b n) -> p b n", b=HALVES).unsqueeze(1).to_broadcast([P, RU, HALVES, P])

            def shift_rows(unit, u, source, first):
                if not first:
                    dve.wait_ge(rows_used, unit - (UB - 1))
                nc.vector.tensor_tensor(shifted[:, u, :, :, 0:P],
                                        source.rearrange("p (r b n) -> p r b n", r=RU, b=HALVES),
                                        shift_r, ALU.subtract).then_inc(rows_ready, 1)

            dve.wait_ge(way_chosen, 1)
            dve.wait_ge(consts_ready, consts)
            with dve.If(dve.value_load(near_zero[0:1, 0:1], min_val=0, max_val=1) == 1):
                nc.vector.memset(shift_col[:, :], 0.0).then_inc(offsets_ready, 1)
                for unit in range(UNITS * KEPT):
                    c, part = unit // UNITS, unit % UNITS
                    split_low(unit, unit % UB, kept[:, c, part * RU * C:(part + 1) * RU * C])
                for j in range(lap_units):
                    s, part = j // UNITS, j % UNITS
                    split_low(UNITS * KEPT + j, (UNITS * KEPT + j) % UB,
                              ring[:, s, part * RU * C:(part + 1) * RU * C])
                with dve.Fori(0, (rounds - 1) // UB) as k:
                    for j in range(UB * lap_units):
                        s, part = j // UNITS % RING, j % UNITS
                        split_low(k * (UB * lap_units) + (head_units + j), (head_units + j) % UB,
                                  ring[:, s, part * RU * C:(part + 1) * RU * C])
                dve.wait_ge(rows_used, units)
                nc.vector.tensor_scalar(cross_half[:, :, :], cross_ps[:, :, 0:P], 0.5, None,
                                        ALU.mult).then_inc(half_ready, 1)
                dve.wait_ge(half_ready, 1)
                nc.vector.tensor_tensor(cross[:, :, :], cross_ps[:, :, P:2 * P], cross_half[:, :, :],
                                        ALU.add).then_inc(cross_ready, 1)
                nc.vector.tensor_copy(high_sum[:, :], cross_ps[:, :, 2 * P]).then_inc(offsets_ready, 1)
                dve.wait_ge(cross_added, 1)
            with dve.Else():
                nc.vector.memset(high_sum[:, :], 0.0).then_inc(offsets_ready, 1)
                nc.vector.tensor_tensor(shift_diag[:, :, :], shift.rearrange("p (b n) -> p b n", b=HALVES),
                                        ident[:, :].unsqueeze(1).to_broadcast([P, HALVES, P]),
                                        ALU.mult).then_inc(shift_diag_ready, 1)
                dve.wait_ge(shift_diag_ready, 1)
                nc.vector.tensor_reduce(shift_col[:, :], shift_diag[:, :, :], AX.X,
                                        ALU.add).then_inc(offsets_ready, 1)
                for unit in range(UNITS * KEPT):
                    c, part = unit // UNITS, unit % UNITS
                    dve.wait_ge(kept_loaded[c], 16)
                    shift_rows(unit, unit % UB, kept[:, c, part * RU * C:(part + 1) * RU * C], unit < UB)
                for j in range(lap_units):
                    s, part = j // UNITS, j % UNITS
                    dve.wait_ge(ring_loaded[s], 16)
                    shift_rows(UNITS * KEPT + j, (UNITS * KEPT + j) % UB,
                               ring[:, s, part * RU * C:(part + 1) * RU * C], False)
                with dve.Fori(0, (rounds - 1) // UB) as k:
                    for j in range(UB * lap_units):
                        s, part, lap = j // UNITS % RING, j % UNITS, j // lap_units
                        dve.wait_ge(ring_loaded[s], k * (16 * UB) + 16 * (lap + 2))
                        shift_rows(k * (UB * lap_units) + (head_units + j), (head_units + j) % UB,
                                   ring[:, s, part * RU * C:(part + 1) * RU * C], False)
                dve.wait_ge(rows_used, units)

            dve.wait_ge(offsets_ready, 2)
            for h in range(PAIR):
                block_h = slice(h * M, (h + 1) * M)
                nc.vector.tensor_copy(moments[block_h, :, 0:M], moments_ps[block_h, :, block_h])
            link(nc.vector.tensor_tensor(moments[:, :, M], moments_ps[:, :, P], high_sum[:, :], ALU.add))
            nc.vector.tensor_tensor(sum_diag[:, :, :], identc[:, :, :],
                                    moments[:, :, M:M + 1].to_broadcast([P, HALVES, M]),
                                    ALU.mult).then_inc(sum_diag_ready, 1)
            nc.vector.scalar_tensor_tensor(out=neg_mean[:, :], in0=moments[:, :, M], scalar=-1.0 / rows,
                                           in1=shift_col[:, :], op0=ALU.mult,
                                           op1=ALU.subtract).then_inc(mean_ready, 1)
            link(nc.vector.tensor_scalar(mean_col[:, :], moments[:, :, M], 1.0 / rows, None, ALU.mult))
            dve.wait_ge(sums_spread, 1)
            for b in range(HALVES):
                last = nc.vector.scalar_tensor_tensor(out=cov[:, b, :], in0=sums_ps[:, b, :],
                                                      scalar=mean_col[:, b:b + 1], in1=moments[:, b, 0:M],
                                                      op0=ALU.mult, op1=ALU.subtract)
            link(last)
            link(nc.vector.scalar_tensor_tensor(out=cov[:, :, :], in0=cov[:, :, :],
                                                scalar=-(1.0 - EPS) / (rows - 1.0), in1=eps_ident[:, :, :],
                                                op0=ALU.mult, op1=ALU.add))
            link(nc.vector.tensor_tensor(cov_diag[:, :, :], cov[:, :, :], identc[:, :, :], ALU.mult))
            nc.vector.tensor_reduce(trace_part[:, :], cov_diag[:, :, :], AX.X,
                                    ALU.add).then_inc(trace_part_ready, 1)
            dve.wait_ge(trace_summed, 1)
            nc.vector.tensor_copy(trace[:, :], trace_ps).then_inc(trace_ready, 1)
            dve.wait_ge(trace_ready, 1)
            link(nc.vector.reciprocal(inv_trace[:, :], trace[:, :]))
            for h in range(PAIR):
                block_h = slice(h * M, (h + 1) * M)
                last = nc.vector.tensor_tensor(sigma[block_h, :, block_h], cov[block_h, :, :],
                                               inv_trace[block_h, :].unsqueeze(2).to_broadcast([M, HALVES, M]),
                                               ALU.mult)
            link(last)

            nc.vector.scalar_tensor_tensor(out=white[:, :, :], in0=sigma[:, :, :], scalar=-0.5,
                                           in1=ident15[:, :, :], op0=ALU.mult,
                                           op1=ALU.add).then_inc(white_ready, 1)
            for t in range(1, ITERATIONS):
                dve.wait_ge(white_ready, t)
                link(nc.vector.tensor_scalar(white15[:, :, :], white[:, :, :], 1.5, None, ALU.mult))
                if t == 1:
                    dve.wait_ge(root_ready, 1)
                    link(nc.vector.reciprocal(newton[:, 0, :], root[:, :]))
                    link(nc.vector.tensor_tensor(newton[:, 1, :], newton[:, 0, :], trace[:, :], ALU.mult))
                    link(nc.vector.tensor_tensor(newton[:, 2, :], newton[:, 1, :], root[:, :], ALU.add))
                    link(nc.vector.tensor_scalar(newton[:, 2, :], newton[:, 2, :], 0.5, None, ALU.mult))
                    link(nc.vector.reciprocal(inv_root[:, :], newton[:, 2, :]))
                dve.wait_ge(products_done, t)
                nc.vector.tensor_copy(products[:, :, :, :], products_ps).then_inc(products_copied, 1)
                dve.wait_ge(cubic_done, t)
                nc.vector.scalar_tensor_tensor(out=white[:, :, :], in0=cubic_ps, scalar=-0.5,
                                               in1=white15[:, :, :], op0=ALU.mult,
                                               op1=ALU.add).then_inc(white_ready, 1)
            dve.wait_ge(white_ready, ITERATIONS)
            dve.wait_ge(params_loaded, 2 * 16)
            for b in range(HALVES):
                last = nc.vector.scalar_tensor_tensor(out=weights[:, b, :], in0=white[:, b, :],
                                                      scalar=inv_root[:, b:b + 1],
                                                      in1=gamma_all[:, b * P:(b + 1) * P],
                                                      op0=ALU.mult, op1=ALU.mult)
            last.then_inc(weights_ready, 1)

            def finish(unit, u, s, part, stores):
                dve.wait_ge(y_summed, unit + 1)
                if part == 0 and stores is not None:
                    dve.wait_ge(y_stored[s], stores)
                nc.vector.tensor_tensor(y[:, s, part * RU * C:(part + 1) * RU * C].rearrange("p (r c) -> p r c", c=C),
                                        y_ps[:, u, :].rearrange("p (r c) -> p r c", c=C),
                                        beta_all[:, :].unsqueeze(1).to_broadcast([P, RU, C]),
                                        ALU.add).then_inc(y_ready, 1)

            for unit in range(2 * RING):
                finish(unit, unit % 2, unit // 2, unit % 2, None)
            with dve.Fori(1, laps) as k:
                for j in range(2 * RING):
                    finish(k * (2 * RING) + j, j % 2, j // 2, j % 2, k * 16)

        @block.tensor
        def _(pe):
            pe.wait_ge(consts_ready, 1)
            pe.wait_ge(squared, 1)
            for r in range(SAMPLE):
                nc.tensor.matmul(sampled_ps[:, 0, :], averager[:, :], kept[:, 0, r * C:(r + 1) * C],
                                 start=(r == 0), stop=(r == SAMPLE - 1))
            for r in range(SAMPLE):
                last = nc.tensor.matmul(sampled_ps[:, 1, :], averager[:, :], squares[:, r * C:(r + 1) * C],
                                        start=(r == 0), stop=(r == SAMPLE - 1))
            last.then_inc(sample_summed, 1)

            def multiply_parts(unit, u, first, final):
                pe.wait_ge(rows_ready, unit + 1)
                for r in range(RU):
                    for b in range(HALVES):
                        nc.tensor.matmul(cross_ps[:, b, :], parts[:, u, r, b, 0:P], parts[:, u, r, b, :],
                                         start=(first and r == 0), stop=(final and r == RU - 1))
                for r in range(RU):
                    for b in range(HALVES):
                        last = nc.tensor.matmul(moments_ps[:, b, :], low_bf16[:, u, r, b, 0:P],
                                                low_bf16[:, u, r, b, 0:P + 1],
                                                start=(first and r == 0), stop=False)
                last.then_inc(rows_used, 1)

            def multiply_shifted(unit, u, first, final):
                pe.wait_ge(rows_ready, unit + 1)
                for r in range(RU):
                    for b in range(HALVES):
                        last = nc.tensor.matmul(moments_ps[:, b, :], shifted[:, u, r, b, 0:P],
                                                shifted[:, u, r, b, :],
                                                start=(first and r == 0), stop=(final and r == RU - 1))
                last.then_inc(rows_used, 1)

            pe.wait_ge(consts_ready, consts)
            pe.wait_ge(way_chosen, 1)
            with pe.If(pe.value_load(near_zero[0:1, 0:1], min_val=0, max_val=1) == 1):
                multiply_parts(0, 0, True, False)
                with pe.Fori(0, (units - 2) // UB) as k:
                    for j in range(UB):
                        multiply_parts(k * UB + (j + 1), (j + 1) % UB, False, False)
                multiply_parts(units - 1, (units - 1) % UB, False, True)
                pe.wait_ge(cross_ready, 1)
                for b in range(HALVES):
                    nc.tensor.matmul(moments_ps[:, b, 0:P], cross[:, b, :], ident[:, :],
                                     start=False, stop=False)
                    last = nc.tensor.matmul(moments_ps[:, b, 0:P], ident[:, :], cross[:, b, :],
                                            start=False, stop=True)
                last.then_inc(cross_added, 1)
            with pe.Else():
                multiply_shifted(0, 0, True, False)
                with pe.Fori(0, (units - 2) // UB) as k:
                    for j in range(UB):
                        multiply_shifted(k * UB + (j + 1), (j + 1) % UB, False, False)
                multiply_shifted(units - 1, (units - 1) % UB, False, True)

            def transpose_unit(unit, u, s, part, loads, first):
                if part == 0:
                    pe.wait_ge(ring_loaded[s], loads)
                if not first:
                    pe.wait_ge(zT_ready, unit - 1)
                for r in range(RU):
                    for b in range(HALVES):
                        col = (part * RU + r) * C + b * P
                        last = nc.tensor.transpose(xT_ps[:, u, b, r * P:(r + 1) * P],
                                                   ring[:, s, col:col + P], ident[:, :])
                last.then_inc(xT_done, 1)

            def multiply_unit(unit, u, first):
                pe.wait_ge(zT_ready, unit + 1)
                if not first:
                    pe.wait_ge(y_ready, unit - 1)
                for r in range(RU):
                    for b in range(HALVES):
                        col = r * C + b * P
                        last = nc.tensor.matmul(y_ps[:, u, col:col + P], zT[:, u, b, r * P:(r + 1) * P],
                                                weights[:, b, :], start=True, stop=True)
                last.then_inc(y_summed, 1)

            transpose_unit(0, 0, 0, 0, 16 * rounds, True)

            pe.wait_ge(sum_diag_ready, 1)
            nc.tensor.matmul(sums_ps.rearrange("p b m -> p (b m)"), same_group[:, :],
                             sum_diag[:, :, :].rearrange("p b m -> p (b m)"),
                             start=True, stop=True).then_inc(sums_spread, 1)
            pe.wait_ge(trace_part_ready, 1)
            nc.tensor.matmul(trace_ps, same_group[:, :], trace_part[:, :],
                             start=True, stop=True).then_inc(trace_summed, 1)
            for t in range(1, ITERATIONS):
                pe.wait_ge(white_ready, t)
                for b in range(HALVES):
                    nc.tensor.matmul(products_ps[:, 0, b, :], white[:, b, :], white[:, b, :],
                                     start=True, stop=True)
                    last = nc.tensor.matmul(products_ps[:, 1, b, :], white[:, b, :], sigma[:, b, :],
                                            start=True, stop=True)
                last.then_inc(products_done, 1)
                pe.wait_ge(products_copied, t)
                for b in range(HALVES):
                    last = nc.tensor.matmul(cubic_ps[:, b, :], products[:, 0, b, :], products[:, 1, b, :],
                                            start=True, stop=True)
                last.then_inc(cubic_done, 1)
            pe.wait_ge(weights_ready, 1)

            def lap(k, first, final):
                for j in range(2 * RING):
                    n = j + 1
                    ahead = k * (2 * RING) + n
                    s, part = (n // 2) % RING, n % 2
                    if not (final and n == 2 * RING):
                        transpose_unit(ahead, n % 2, s, part,
                                       k * 16 + 16 * (rounds + n // (2 * RING)), first and n < 2)
                    multiply_unit(k * (2 * RING) + j, j % 2, first and j < 2)

            lap(0, True, False)
            with pe.Fori(1, laps - 1) as k:
                lap(k, False, False)
            lap(laps - 1, False, True)


def kernel(x, L0_conv_gamma, L0_conv_beta):
    import numpy as _np
    import concourse.bacc as _bacc
    from concourse import mybir as _mybir
    from concourse.bass_utils import run_bass_kernel_spmd as _run

    nc = _bacc.Bacc("TRN2", target_bir_lowering=False, num_devices=1)
    arrays, args = {}, []
    for name, value in (("x", x), ("gamma", L0_conv_gamma), ("beta", L0_conv_beta)):
        a = _np.ascontiguousarray(value)
        arrays[name] = a
        args.append(nc.dram_tensor(name, a.shape, _mybir.dt.from_np(a.dtype), kind="ExternalInput").ap())
    args.append(nc.dram_tensor("out", arrays["x"].shape, _mybir.dt.float32, kind="ExternalOutput").ap())
    build(nc, *args)
    r = _run(nc, [arrays], core_ids=[0])
    return r.results[0]["out"]
```

```python
import concourse.bass as bass
from concourse import mybir
from contextlib import ExitStack

FP32 = mybir.dt.float32
FP32R = mybir.dt.float32r
BF16 = mybir.dt.bfloat16
INT32 = mybir.dt.int32
ALU = mybir.AluOpType
ACT = mybir.ActivationFunctionType
AX = mybir.AxisListType

P = 128
C = 256
M = 64
HALVES = C // P
PAIR = P // M
RP = 8
CHUNK = P * RP
UNITS = 2
RU = RP // UNITS
RING = 4
KEPT = 16
UB = 3
AHEAD = 4
YB = RING
EARLY = 2
LEAD = RING + 1
SCRATCH = 3392
SAMPLE = 1
OFFSET = 16.0
EPS = 1e-5
ITERATIONS = 5


def build(nc: bass.Bass, x, gamma, beta, out):
    rows = x.shape[0] * x.shape[1] * x.shape[2]
    chunks = rows // CHUNK
    passed = chunks - KEPT
    rounds = passed // RING
    units = UNITS * chunks
    lap_units = UNITS * RING
    head_laps = (rounds - 1) % UB + 1
    head_units = UNITS * KEPT + head_laps * lap_units
    loop_units = UB * lap_units
    laps = chunks // RING
    span = (chunks - RING) // KEPT
    assert (units - 2) % UB == 0
    assert chunks * CHUNK == rows and rounds * RING == passed and laps * RING == chunks
    assert span * KEPT == chunks - RING and span % RING == 0

    x_v = x.rearrange("b h w c -> (b h w) c").rearrange("(i p r) c -> i p (r c)", p=P, r=RP)
    out_v = out.rearrange("b h w c -> (b h w) c").rearrange("(i p r) c -> i p (r c)", p=P, r=RP)
    gamma_v = gamma.rearrange("a b c d -> (a b c) d")
    beta_v = beta.rearrange("a b c d -> (a b c) d")

    ctx = ExitStack()
    with ctx:
        def sb(name, shape, dtype=FP32):
            return ctx.enter_context(nc.sbuf_tensor(name, shape, dtype))

        def sem(name):
            return ctx.enter_context(nc.semaphore(name))

        ring = sb("ring", [P, RING, RP * C])
        kept = sb("kept", [P, KEPT, RP * C])
        with ExitStack() as first_pass:
            parts = first_pass.enter_context(
                nc.sbuf_tensor("parts", [P, UB, RU, HALVES, 2 * P + 2], FP32R))
            low_bf16 = parts[:, :, :, :, :].bitcast(BF16)\
                .rearrange("p u r b (n t) -> p u r b n t", t=2)[:, :, :, :, P:, 1]
            scratch_all = first_pass.enter_context(nc.sbuf_tensor("scratch", [P, SCRATCH], FP32))
        with ExitStack() as other_way:
            shifted = other_way.enter_context(
                nc.sbuf_tensor("shifted", [P, UB, RU, HALVES, P + 1], FP32))
        zT = sb("zT", [P, 2, HALVES, RU * P])
        y = sb("y", [P, YB, RP * C])
        assert HALVES * 2 * RU * P + EARLY * RP * C <= UB * RU * HALVES * (2 * P + 2)

        def y_slot(s):
            return (s + EARLY) % YB

        carved = [0]

        def scratch(shape):
            first, size = carved[0], shape[1] * shape[2]
            carved[0] += size
            assert carved[0] <= SCRATCH
            return scratch_all[:, first:first + size].rearrange("p (a b) -> p a b", b=shape[2])

        ident = sb("ident", [P, P])
        identc = sb("identc", [P, 1, M])
        eps_ident = sb("eps_ident", [P, 1, M])
        ident15 = sb("ident15", [P, 1, P])
        same_group = sb("same_group", [P, P])
        averager = scratch([P, 1, P])[:, 0, :]
        gamma_all = sb("gamma_all", [P, C])
        beta_all = sb("beta_all", [P, C])
        shift_all = sb("shift", [P, C])
        shift = shift_all[:, :]
        mean_sq = scratch([P, 1, C])[:, 0, :]
        margin = scratch([P, 1, C])[:, 0, :]
        squares = scratch([P, SAMPLE, C])
        least_margin = sb("least_margin", [P, 1])
        near_zero = sb("near_zero", [P, 1], INT32)
        cross_half = scratch([P, HALVES, P])
        cross = scratch([P, HALVES, P])
        high_sum = sb("high_sum", [P, HALVES])
        shift_diag = scratch([P, HALVES, P])
        shift_col = sb("shift_col", [P, HALVES])
        moments = sb("moments", [P, HALVES, M + 1])
        sum_diag = scratch([P, HALVES, M])
        mean_col = sb("mean_col", [P, HALVES])
        neg_mean = sb("neg_mean", [P, HALVES])
        cov = scratch([P, HALVES, M])
        cov_diag = scratch([P, HALVES, M])
        trace_part = sb("trace_part", [P, HALVES])
        trace = sb("trace", [P, HALVES])
        inv_trace = sb("inv_trace", [P, HALVES])
        root = sb("root", [P, HALVES])
        newton = sb("newton", [P, 3, HALVES])
        inv_root = sb("inv_root", [P, HALVES])
        sigma = scratch([P, HALVES, P])
        white = scratch([P, HALVES, P])
        white15 = scratch([P, HALVES, P])
        products = scratch([P, 2 * HALVES, P]).rearrange("p (k b) n -> p k b n", k=2)
        weights = sb("weights", [P, HALVES, P])

        banks = ctx.enter_context(nc.psum_tensor("banks", [P, 8, 512], FP32))
        xT_ps = banks[:, 0:4, :].rearrange("p (u b) n -> p u b n", u=2)
        y_ps = banks[:, 4:8, :].rearrange("p (u v) n -> p u (v n)", u=2)
        moments_ps = banks[:, 4:6, 0:P + 1]
        cross_ps = banks[:, 6:8, 0:2 * P + 2]
        sampled_ps = banks[:, 2:4, 0:C]
        sums_ps = banks[:, 6, 0:P].rearrange("p (b m) -> p b m", b=HALVES)
        trace_ps = banks[:, 7, 0:HALVES]
        products_ps = banks[:, 6, :].rearrange("p (k b n) -> p k b n", k=2, b=HALVES)
        cubic_ps = banks[:, 7, 0:HALVES * P].rearrange("p (b n) -> p b n", b=HALVES)

        ring_loaded = [sem(f"ring_loaded{s}") for s in range(RING)]
        kept_loaded = [sem(f"kept_loaded{k}") for k in range(KEPT)]
        params_loaded = sem("params_loaded")
        consts_ready = sem("consts_ready")
        sample_loaded = sem("sample_loaded")
        squared = sem("squared")
        sample_summed = sem("sample_summed")
        way_chosen = sem("way_chosen")
        high_ready = sem("high_ready")
        rows_ready = sem("rows_ready")
        rows_used = sem("rows_used")
        shift_diag_ready = sem("shift_diag_ready")
        ones_set = sem("ones_set")
        half_ready = sem("half_ready")
        cross_ready = sem("cross_ready")
        cross_added = sem("cross_added")
        offsets_ready = sem("offsets_ready")
        sum_diag_ready = sem("sum_diag_ready")
        sums_spread = sem("sums_spread")
        trace_part_ready = sem("trace_part_ready")
        trace_summed = sem("trace_summed")
        trace_ready = sem("trace_ready")
        root_ready = sem("root_ready")
        mean_ready = sem("mean_ready")
        white_ready = sem("white_ready")
        products_done = sem("products_done")
        products_copied = sem("products_copied")
        cubic_done = sem("cubic_done")
        weights_ready = sem("weights_ready")
        chain = sem("chain")
        xT_done = sem("xT_done")
        zT_ready = sem("zT_ready")
        y_summed = sem("y_summed")
        y_ready = sem("y_ready")
        early_loaded = [sem(f"early_loaded{e}") for e in range(EARLY)]
        y_stored = [sem(f"y_stored{s}") for s in range(YB)]

        early_slot = [RING - EARLY + e for e in range(EARLY)]

        block = ctx.enter_context(nc.Block())

        @block.sync
        def _(sp):
            sp.dma_start(kept[:, 0, 0:SAMPLE * C], x_v[0][:, 0:SAMPLE * C]).then_inc(sample_loaded, 16)
            sp.dma_start(kept[:, 0, SAMPLE * C:], x_v[0][:, SAMPLE * C:]).then_inc(kept_loaded[0], 16)
            for c in range(1, KEPT):
                sp.dma_start(kept[:, c, :], x_v[c]).then_inc(kept_loaded[c], 16)
            for s in range(RING):
                sp.dma_start(ring[:, s, :], x_v[KEPT + s]).then_inc(ring_loaded[s], 16)
            sp.dma_start(gamma_all[:, :], gamma_v.partition_broadcast(P)).then_inc(params_loaded, 16)
            sp.dma_start(beta_all[:, :], beta_v.partition_broadcast(P)).then_inc(params_loaded, 16)
            with sp.Fori(1, rounds) as k:
                for s in range(RING):
                    sp.wait_ge(rows_ready, k * lap_units + UNITS * (KEPT - RING + s + 1))
                    sp.dma_start(ring[:, s, :], x_v[k * RING + (KEPT + s)]).then_inc(ring_loaded[s], 16)

            def store(position, s, chunk):
                sp.wait_ge(y_ready, 2 * position + 2)
                sp.dma_start(out_v[chunk], y[:, y_slot(s), :]).then_inc(y_stored[y_slot(s)], 16)

            def load(position, s, chunk):
                sp.wait_ge(xT_done, 2 * (position - RING + 1))
                sp.dma_start(ring[:, s, :], x_v[chunk]).then_inc(ring_loaded[s], 16)

            sp.wait_ge(rows_used, units)
            for e in range(EARLY):
                sp.dma_start(y[:, e, :], x_v[KEPT + early_slot[e]]).then_inc(early_loaded[e], 16)
            load(RING, 0, KEPT)
            for s in range(RING):
                if (LEAD + s) % RING not in early_slot:
                    load(LEAD + s, (LEAD + s) % RING, KEPT + s + 1)
                store(s, s, chunks - RING + s)
            with sp.Fori(0, KEPT - 1) as run:
                for j in range(span):
                    ahead = j + LEAD
                    if ahead < span - 1:
                        load(run * span + (RING + ahead), ahead % RING,
                             run * (span - 1) + (KEPT + ahead))
                    elif ahead >= span:
                        load(run * span + (RING + ahead), ahead % RING,
                             run * (span - 1) + (KEPT + span - 1 + ahead - span))
                    store(run * span + (RING + j), j % RING,
                          run * (span - 1) + (KEPT + j) if j < span - 1 else run)
            last = KEPT - 1
            for j in range(span):
                ahead = j + LEAD
                if ahead < span - 1:
                    load(last * span + RING + ahead, ahead % RING,
                         KEPT + last * (span - 1) + ahead)
                store(last * span + RING + j, j % RING,
                      KEPT + last * (span - 1) + j if j < span - 1 else last)
            for s in range(YB):
                sp.wait_ge(y_stored[s], 16 * (chunks // YB))

        consts = 1 + UB + 4 + PAIR + 1 + 2 * PAIR

        @block.gpsimd
        def _(pool):
            made = [0]

            def make(ins):
                made[0] += 1
                ins.then_inc(consts_ready, 1)
                pool.wait_ge(consts_ready, made[0])

            make(pool.memset(averager, 1.0 / (P * SAMPLE)))
            for u in range(UB):
                make(pool.memset(parts[:, u, :, :, 2 * P:].bitcast(FP32), 1.0))
            make(pool.memset(ident[:, :], 0.0))
            make(pool.affine_select(out=ident[:, :], in_=ident[:, :], compare_op=ALU.not_equal, fill=1.0,
                                    base=0, pattern=[[-1, P]], channel_multiplier=1))
            make(pool.memset(sigma[:, :, :], 0.0))
            make(pool.memset(same_group[:, :], 0.0))
            for h in range(PAIR):
                block_h = slice(h * M, (h + 1) * M)
                make(pool.memset(same_group[block_h, block_h], 1.0))
            make(pool.tensor_scalar(ident15[:, 0, :], ident[:, :], 1.5, None, ALU.mult))
            for h in range(PAIR):
                block_h = slice(h * M, (h + 1) * M)
                make(pool.tensor_scalar(identc[block_h, 0, :], ident[block_h, block_h], 1.0, None,
                                        ALU.mult))
                make(pool.tensor_scalar(eps_ident[block_h, 0, :], ident[block_h, block_h], EPS, None,
                                        ALU.mult))
            assert made[0] == consts
            for c in range(KEPT):
                position = RING + (c + 1) * span - 1
                s = position % RING
                pool.wait_ge(kept_loaded[c], 16)
                pool.wait_ge(xT_done, 2 * (position - RING + 1))
                pool.tensor_copy(ring[:, s, :], kept[:, c, :]).then_inc(ring_loaded[s], 16)

        @block.scalar
        def _(act):
            act.wait_ge(sample_loaded, 16)
            nc.scalar.activation(squares.rearrange("p r c -> p (r c)"), kept[:, 0, 0:SAMPLE * C],
                                 ACT.Square).then_inc(squared, 1)

            def split_high(unit, u, source, first):
                if not first:
                    act.wait_ge(rows_used, unit - (UB - 1))
                nc.scalar.activation(parts[:, u, :, :, 0:P],
                                     source.rearrange("p (r b n) -> p r b n", r=RU, b=HALVES),
                                     ACT.Copy).then_inc(high_ready, 1)

            act.wait_ge(way_chosen, 1)
            with act.If(act.value_load(near_zero[0:1, 0:1], min_val=0, max_val=1) == 1):
                for unit in range(UNITS * KEPT):
                    c, part = unit // UNITS, unit % UNITS
                    act.wait_ge(kept_loaded[c], 16)
                    split_high(unit, unit % UB, kept[:, c, part * RU * C:(part + 1) * RU * C], unit < UB)
                for j in range(head_laps * lap_units):
                    s, part, lap = j // UNITS % RING, j % UNITS, j // lap_units
                    act.wait_ge(ring_loaded[s], 16 * (lap + 1))
                    split_high(UNITS * KEPT + j, (UNITS * KEPT + j) % UB,
                               ring[:, s, part * RU * C:(part + 1) * RU * C], False)
                with act.Fori(0, (rounds - head_laps) // UB) as k:
                    for j in range(loop_units):
                        s, part, lap = j // UNITS % RING, j % UNITS, j // lap_units
                        act.wait_ge(ring_loaded[s], k * (16 * UB) + 16 * (head_laps + lap + 1))
                        split_high(k * loop_units + (head_units + j), (head_units + j) % UB,
                                   ring[:, s, part * RU * C:(part + 1) * RU * C], False)

            def center(unit, u, first):
                act.wait_ge(xT_done, unit + 1)
                if not first:
                    act.wait_ge(y_summed, unit - 1)
                for b in range(HALVES):
                    last = nc.scalar.activation(zT[:, u, b, :], xT_ps[:, u, b, :], ACT.Identity,
                                                bias=neg_mean[:, b:b + 1])
                last.then_inc(zT_ready, 1)

            act.wait_ge(mean_ready, 1)
            for unit in range(2):
                center(unit, unit % 2, True)
            act.wait_ge(trace_ready, 1)
            nc.scalar.activation(root[:, :], trace[:, :], ACT.Sqrt).then_inc(root_ready, 1)
            for unit in range(2, 2 * RING):
                center(unit, unit % 2, False)
            with act.Fori(1, laps) as k:
                for j in range(2 * RING):
                    center(k * (2 * RING) + j, j % 2, False)

        @block.vector
        def _(dve):
            links = [0]

            def link(ins):
                links[0] += 1
                ins.then_inc(chain, 1)
                dve.wait_ge(chain, links[0])

            dve.wait_ge(sample_summed, 1)
            link(nc.vector.tensor_copy(shift, sampled_ps[:, 0, :]))
            link(nc.vector.scalar_tensor_tensor(out=mean_sq, in0=shift, scalar=1.0 + OFFSET,
                                                in1=shift, op0=ALU.mult, op1=ALU.mult))
            link(nc.vector.scalar_tensor_tensor(out=margin, in0=sampled_ps[:, 1, :], scalar=OFFSET,
                                                in1=mean_sq, op0=ALU.mult, op1=ALU.subtract))
            link(nc.vector.tensor_reduce(least_margin[:, :], margin, AX.X, ALU.min))
            nc.vector.tensor_scalar(near_zero[:, :], least_margin[:, :], 0.0, None, ALU.is_ge)\
                .then_inc(way_chosen, 1)

            def split_low(unit, u, source):
                dve.wait_ge(high_ready, unit + 1)
                nc.vector.tensor_tensor(parts[:, u, :, :, P:2 * P],
                                        source.rearrange("p (r b n) -> p r b n", r=RU, b=HALVES),
                                        parts[:, u, :, :, 0:P], ALU.subtract).then_inc(rows_ready, 1)

            shift_r = shift.rearrange("p (b n) -> p b n", b=HALVES).unsqueeze(1)\
                .to_broadcast([P, RU, HALVES, P])

            def shift_rows(unit, u, source, first):
                if not first:
                    dve.wait_ge(rows_used, unit - (UB - 1))
                nc.vector.tensor_tensor(shifted[:, u, :, :, 0:P],
                                        source.rearrange("p (r b n) -> p r b n", r=RU, b=HALVES),
                                        shift_r, ALU.subtract).then_inc(rows_ready, 1)

            dve.wait_ge(way_chosen, 1)
            dve.wait_ge(consts_ready, consts)
            with dve.If(dve.value_load(near_zero[0:1, 0:1], min_val=0, max_val=1) == 1):
                nc.vector.memset(shift_col[:, :], 0.0).then_inc(offsets_ready, 1)
                for unit in range(UNITS * KEPT):
                    c, part = unit // UNITS, unit % UNITS
                    split_low(unit, unit % UB, kept[:, c, part * RU * C:(part + 1) * RU * C])
                for j in range(head_laps * lap_units):
                    s, part, lap = j // UNITS % RING, j % UNITS, j // lap_units
                    split_low(UNITS * KEPT + j, (UNITS * KEPT + j) % UB,
                              ring[:, s, part * RU * C:(part + 1) * RU * C])
                with dve.Fori(0, (rounds - head_laps) // UB) as k:
                    for j in range(loop_units):
                        s, part = j // UNITS % RING, j % UNITS
                        split_low(k * loop_units + (head_units + j), (head_units + j) % UB,
                                  ring[:, s, part * RU * C:(part + 1) * RU * C])
                dve.wait_ge(rows_used, units)
                nc.vector.tensor_scalar(cross_half[:, :, :], cross_ps[:, :, 0:P], 0.5, None,
                                        ALU.mult).then_inc(half_ready, 1)
                dve.wait_ge(half_ready, 1)
                nc.vector.tensor_tensor(cross[:, :, :], cross_ps[:, :, P:2 * P], cross_half[:, :, :],
                                        ALU.add).then_inc(cross_ready, 1)
                nc.vector.tensor_copy(high_sum[:, :], cross_ps[:, :, 2 * P]).then_inc(offsets_ready, 1)
                dve.wait_ge(cross_added, 1)
            with dve.Else():
                nc.vector.memset(high_sum[:, :], 0.0).then_inc(offsets_ready, 1)
                nc.vector.memset(shifted[:, :, :, :, P:], 1.0).then_inc(ones_set, 1)
                dve.wait_ge(ones_set, 1)
                nc.vector.tensor_tensor(shift_diag[:, :, :], shift.rearrange("p (b n) -> p b n", b=HALVES),
                                        ident[:, :].unsqueeze(1).to_broadcast([P, HALVES, P]),
                                        ALU.mult).then_inc(shift_diag_ready, 1)
                dve.wait_ge(shift_diag_ready, 1)
                nc.vector.tensor_reduce(shift_col[:, :], shift_diag[:, :, :], AX.X,
                                        ALU.add).then_inc(offsets_ready, 1)
                for unit in range(UNITS * KEPT):
                    c, part = unit // UNITS, unit % UNITS
                    dve.wait_ge(kept_loaded[c], 16)
                    shift_rows(unit, unit % UB, kept[:, c, part * RU * C:(part + 1) * RU * C], unit < UB)
                for j in range(head_laps * lap_units):
                    s, part, lap = j // UNITS % RING, j % UNITS, j // lap_units
                    dve.wait_ge(ring_loaded[s], 16 * (lap + 1))
                    shift_rows(UNITS * KEPT + j, (UNITS * KEPT + j) % UB,
                               ring[:, s, part * RU * C:(part + 1) * RU * C], False)
                with dve.Fori(0, (rounds - head_laps) // UB) as k:
                    for j in range(loop_units):
                        s, part, lap = j // UNITS % RING, j % UNITS, j // lap_units
                        dve.wait_ge(ring_loaded[s], k * (16 * UB) + 16 * (head_laps + lap + 1))
                        shift_rows(k * loop_units + (head_units + j), (head_units + j) % UB,
                                   ring[:, s, part * RU * C:(part + 1) * RU * C], False)
                dve.wait_ge(rows_used, units)

            dve.wait_ge(offsets_ready, 2)
            for h in range(PAIR):
                block_h = slice(h * M, (h + 1) * M)
                nc.vector.tensor_copy(moments[block_h, :, 0:M], moments_ps[block_h, :, block_h])
            link(nc.vector.tensor_tensor(moments[:, :, M], moments_ps[:, :, P], high_sum[:, :], ALU.add))
            nc.vector.tensor_tensor(sum_diag[:, :, :], identc[:, :, :].to_broadcast([P, HALVES, M]),
                                    moments[:, :, M:M + 1].to_broadcast([P, HALVES, M]),
                                    ALU.mult).then_inc(sum_diag_ready, 1)
            nc.vector.scalar_tensor_tensor(out=neg_mean[:, :], in0=moments[:, :, M], scalar=-1.0 / rows,
                                           in1=shift_col[:, :], op0=ALU.mult,
                                           op1=ALU.subtract).then_inc(mean_ready, 1)
            link(nc.vector.tensor_scalar(mean_col[:, :], moments[:, :, M], 1.0 / rows, None, ALU.mult))
            dve.wait_ge(sums_spread, 1)
            for b in range(HALVES):
                last = nc.vector.scalar_tensor_tensor(out=cov[:, b, :], in0=sums_ps[:, b, :],
                                                      scalar=mean_col[:, b:b + 1], in1=moments[:, b, 0:M],
                                                      op0=ALU.mult, op1=ALU.subtract)
            link(last)
            link(nc.vector.scalar_tensor_tensor(out=cov[:, :, :], in0=cov[:, :, :],
                                                scalar=-(1.0 - EPS) / (rows - 1.0),
                                                in1=eps_ident[:, :, :].to_broadcast([P, HALVES, M]),
                                                op0=ALU.mult, op1=ALU.add))
            link(nc.vector.tensor_tensor(cov_diag[:, :, :], cov[:, :, :],
                                         identc[:, :, :].to_broadcast([P, HALVES, M]), ALU.mult))
            nc.vector.tensor_reduce(trace_part[:, :], cov_diag[:, :, :], AX.X,
                                    ALU.add).then_inc(trace_part_ready, 1)
            dve.wait_ge(trace_summed, 1)
            nc.vector.tensor_copy(trace[:, :], trace_ps).then_inc(trace_ready, 1)
            dve.wait_ge(trace_ready, 1)
            link(nc.vector.reciprocal(inv_trace[:, :], trace[:, :]))
            for h in range(PAIR):
                block_h = slice(h * M, (h + 1) * M)
                last = nc.vector.tensor_tensor(sigma[block_h, :, block_h], cov[block_h, :, :],
                                               inv_trace[block_h, :].unsqueeze(2).to_broadcast([M, HALVES, M]),
                                               ALU.mult)
            link(last)

            nc.vector.scalar_tensor_tensor(out=white[:, :, :], in0=sigma[:, :, :], scalar=-0.5,
                                           in1=ident15[:, :, :].to_broadcast([P, HALVES, P]), op0=ALU.mult,
                                           op1=ALU.add).then_inc(white_ready, 1)
            for t in range(1, ITERATIONS):
                dve.wait_ge(white_ready, t)
                link(nc.vector.tensor_scalar(white15[:, :, :], white[:, :, :], 1.5, None, ALU.mult))
                if t == 1:
                    dve.wait_ge(root_ready, 1)
                    link(nc.vector.reciprocal(newton[:, 0, :], root[:, :]))
                    link(nc.vector.tensor_tensor(newton[:, 1, :], newton[:, 0, :], trace[:, :], ALU.mult))
                    link(nc.vector.tensor_tensor(newton[:, 2, :], newton[:, 1, :], root[:, :], ALU.add))
                    link(nc.vector.tensor_scalar(newton[:, 2, :], newton[:, 2, :], 0.5, None, ALU.mult))
                    link(nc.vector.reciprocal(inv_root[:, :], newton[:, 2, :]))
                dve.wait_ge(products_done, t)
                nc.vector.tensor_copy(products[:, :, :, :], products_ps).then_inc(products_copied, 1)
                dve.wait_ge(cubic_done, t)
                nc.vector.scalar_tensor_tensor(out=white[:, :, :], in0=cubic_ps, scalar=-0.5,
                                               in1=white15[:, :, :], op0=ALU.mult,
                                               op1=ALU.add).then_inc(white_ready, 1)
            dve.wait_ge(white_ready, ITERATIONS)
            dve.wait_ge(params_loaded, 2 * 16)
            for b in range(HALVES):
                last = nc.vector.scalar_tensor_tensor(out=weights[:, b, :], in0=white[:, b, :],
                                                      scalar=inv_root[:, b:b + 1],
                                                      in1=gamma_all[:, b * P:(b + 1) * P],
                                                      op0=ALU.mult, op1=ALU.mult)
            last.then_inc(weights_ready, 1)

            def finish(unit, u, s, part, stores):
                dve.wait_ge(y_summed, unit + 1)
                if part == 0 and stores is not None:
                    dve.wait_ge(y_stored[y_slot(s)], stores)
                y_rows = y[:, y_slot(s), part * RU * C:(part + 1) * RU * C].rearrange("p (r c) -> p r c", c=C)
                nc.vector.tensor_tensor(y_rows,
                                        y_ps[:, u, :].rearrange("p (r c) -> p r c", c=C),
                                        beta_all[:, :].unsqueeze(1).to_broadcast([P, RU, C]),
                                        ALU.add).then_inc(y_ready, 1)

            for unit in range(2 * RING):
                s = unit // 2
                if unit % 2 == 0 and s in early_slot:
                    e = early_slot.index(s)
                    dve.wait_ge(early_loaded[e], 16)
                    dve.wait_ge(xT_done, 2 * (s + 1))
                    nc.vector.tensor_copy(ring[:, s, :], y[:, e, :]).then_inc(ring_loaded[s], 16)
                    dve.wait_ge(ring_loaded[s], 16 * (rounds + 1))
                finish(unit, unit % 2, s, unit % 2, None)
            with dve.Fori(1, laps) as k:
                for j in range(2 * RING):
                    finish(k * (2 * RING) + j, j % 2, j // 2, j % 2, k * 16)

        @block.tensor
        def _(pe):
            pe.wait_ge(consts_ready, 1)
            pe.wait_ge(squared, 1)
            for r in range(SAMPLE):
                nc.tensor.matmul(sampled_ps[:, 0, :], averager, kept[:, 0, r * C:(r + 1) * C],
                                 start=(r == 0), stop=(r == SAMPLE - 1))
            for r in range(SAMPLE):
                last = nc.tensor.matmul(sampled_ps[:, 1, :], averager, squares[:, r, :],
                                        start=(r == 0), stop=(r == SAMPLE - 1))
            last.then_inc(sample_summed, 1)

            def multiply_parts(unit, u, first, final):
                pe.wait_ge(rows_ready, unit + 1)
                for r in range(RU):
                    for b in range(HALVES):
                        nc.tensor.matmul(cross_ps[:, b, :], parts[:, u, r, b, 0:P], parts[:, u, r, b, :],
                                         start=(first and r == 0), stop=(final and r == RU - 1))
                for r in range(RU):
                    for b in range(HALVES):
                        last = nc.tensor.matmul(moments_ps[:, b, :], low_bf16[:, u, r, b, 0:P],
                                                low_bf16[:, u, r, b, 0:P + 1],
                                                start=(first and r == 0), stop=False)
                last.then_inc(rows_used, 1)

            def multiply_shifted(unit, u, first, final):
                pe.wait_ge(rows_ready, unit + 1)
                for r in range(RU):
                    for b in range(HALVES):
                        last = nc.tensor.matmul(moments_ps[:, b, :], shifted[:, u, r, b, 0:P],
                                                shifted[:, u, r, b, :],
                                                start=(first and r == 0), stop=(final and r == RU - 1))
                last.then_inc(rows_used, 1)

            pe.wait_ge(consts_ready, consts)
            pe.wait_ge(way_chosen, 1)
            with pe.If(pe.value_load(near_zero[0:1, 0:1], min_val=0, max_val=1) == 1):
                multiply_parts(0, 0, True, False)
                with pe.Fori(0, (units - 2) // UB) as k:
                    for j in range(UB):
                        multiply_parts(k * UB + (j + 1), (j + 1) % UB, False, False)
                multiply_parts(units - 1, (units - 1) % UB, False, True)
                pe.wait_ge(cross_ready, 1)
                for b in range(HALVES):
                    nc.tensor.matmul(moments_ps[:, b, 0:P], cross[:, b, :], ident[:, :],
                                     start=False, stop=False)
                    last = nc.tensor.matmul(moments_ps[:, b, 0:P], ident[:, :], cross[:, b, :],
                                            start=False, stop=True)
                last.then_inc(cross_added, 1)
            with pe.Else():
                multiply_shifted(0, 0, True, False)
                with pe.Fori(0, (units - 2) // UB) as k:
                    for j in range(UB):
                        multiply_shifted(k * UB + (j + 1), (j + 1) % UB, False, False)
                multiply_shifted(units - 1, (units - 1) % UB, False, True)

            def transpose_unit(unit, u, s, part, loads, first):
                if part == 0:
                    pe.wait_ge(ring_loaded[s], loads)
                if not first:
                    pe.wait_ge(zT_ready, unit - 1)
                for r in range(RU):
                    for b in range(HALVES):
                        col = (part * RU + r) * C + b * P
                        last = nc.tensor.transpose(xT_ps[:, u, b, r * P:(r + 1) * P],
                                                   ring[:, s, col:col + P], ident[:, :])
                last.then_inc(xT_done, 1)

            def multiply_unit(unit, u, first):
                pe.wait_ge(zT_ready, unit + 1)
                if not first:
                    pe.wait_ge(y_ready, unit - 1)
                for r in range(RU):
                    for b in range(HALVES):
                        col = r * C + b * P
                        last = nc.tensor.matmul(y_ps[:, u, col:col + P], zT[:, u, b, r * P:(r + 1) * P],
                                                weights[:, b, :], start=True, stop=True)
                last.then_inc(y_summed, 1)

            for unit in range(2):
                transpose_unit(unit, unit, 0, unit, 16 * rounds, True)

            pe.wait_ge(sum_diag_ready, 1)
            nc.tensor.matmul(sums_ps.rearrange("p b m -> p (b m)"), same_group[:, :],
                             sum_diag[:, :, :].rearrange("p b m -> p (b m)"),
                             start=True, stop=True).then_inc(sums_spread, 1)
            pe.wait_ge(trace_part_ready, 1)
            nc.tensor.matmul(trace_ps, same_group[:, :], trace_part[:, :],
                             start=True, stop=True).then_inc(trace_summed, 1)
            transpose_unit(2, 0, 1, 0, 16 * rounds, False)
            for t in range(1, ITERATIONS):
                pe.wait_ge(white_ready, t)
                for b in range(HALVES):
                    nc.tensor.matmul(products_ps[:, 0, b, :], white[:, b, :], white[:, b, :],
                                     start=True, stop=True)
                    last = nc.tensor.matmul(products_ps[:, 1, b, :], white[:, b, :], sigma[:, b, :],
                                            start=True, stop=True)
                last.then_inc(products_done, 1)
                if t == 1:
                    transpose_unit(3, 1, 1, 1, 16 * rounds, False)
                pe.wait_ge(products_copied, t)
                for b in range(HALVES):
                    last = nc.tensor.matmul(cubic_ps[:, b, :], products[:, 0, b, :], products[:, 1, b, :],
                                            start=True, stop=True)
                last.then_inc(cubic_done, 1)
            pe.wait_ge(weights_ready, 1)

            def lap(k, first, final):
                for j in range(2 * RING):
                    n = j + 1
                    ahead = k * (2 * RING) + n
                    s, part = (n // 2) % RING, n % 2
                    if not (first and n < AHEAD or final and n == 2 * RING):
                        transpose_unit(ahead, n % 2, s, part,
                                       k * 16 + 16 * (rounds + n // (2 * RING)), False)
                    multiply_unit(k * (2 * RING) + j, j % 2, first and j < 2)

            lap(0, True, False)
            with pe.Fori(1, laps - 1) as k:
                lap(k, False, False)
            lap(laps - 1, False, True)


def kernel(x, L0_conv_gamma, L0_conv_beta):
    import numpy as _np
    import concourse.bacc as _bacc
    from concourse import mybir as _mybir
    from concourse.bass_utils import run_bass_kernel_spmd as _run

    nc = _bacc.Bacc("TRN2", target_bir_lowering=False, num_devices=1)
    arrays, args = {}, []
    for name, value in (("x", x), ("gamma", L0_conv_gamma), ("beta", L0_conv_beta)):
        a = _np.ascontiguousarray(value)
        arrays[name] = a
        args.append(nc.dram_tensor(name, a.shape, _mybir.dt.from_np(a.dtype), kind="ExternalInput").ap())
    args.append(nc.dram_tensor("out", arrays["x"].shape, _mybir.dt.float32, kind="ExternalOutput").ap())
    build(nc, *args)
    r = _run(nc, [arrays], core_ids=[0])
    return r.results[0]["out"]
```
